# Optimizing a Trainium2 kernel written in Bass

```python
import numpy as np
import jax
import jax.numpy as jnp

def _softmax(x, axis=-1):
    return jax.nn.softmax(x, axis=axis)

def _gelu(x):
    return jax.nn.gelu(x, approximate=True)

def _silu(x):
    return jax.nn.silu(x)

def _sigmoid(x):
    return jax.nn.sigmoid(x)

def _layernorm(x, axis=-1, eps=1e-05):
    m = jnp.mean(x, axis=axis, keepdims=True)
    v = jnp.var(x, axis=axis, keepdims=True)
    return (x - m) / jnp.sqrt(v + eps)

def _scatter_add(tgt, idx, src, axis=0):
    return tgt.at[idx].add(src)

def _segment_sum(src, seg, n):
    return jax.ops.segment_sum(src, seg, n)
kernel_name = 'mk_adj_ffn_d1_adj_r2_1a37ab'

def setup_inputs(seed: int=0):
    np.random.seed(seed)
    _w = jnp.asarray

    def _rec_inputs():
        import jax
        import jax.numpy as jnp
        _gk = jax.random.key(seed)
        x = -0.0002422 + 1 * jax.random.normal(jax.random.fold_in(_gk, 1), (128, 128, 128), jnp.float32)
        _a = jax.random.bernoulli(jax.random.fold_in(_gk, 2), 0.125, (128, 128, 128))
        _a = jnp.logical_or(_a, jnp.swapaxes(_a, -1, -2))
        _a = jnp.logical_or(_a, jnp.eye(128, dtype=bool))
        adj = _a.astype(jnp.int32)
        return (x, adj)
    x, adj = _rec_inputs()

    def _L0_gnn_setup():
        import jax, jax.numpy as jnp
        import numpy as np
        NEG_INF = -9000000000000000.0
        LEAKY_SLOPE = 0.2
        key = jax.random.key(seed)
        k1, k2, k3, k4, k5, k6 = jax.random.split(key, 6)
        B, N, D = (256, 200, 128)
        hidden = jax.random.normal(k1, (B, N, D), dtype=jnp.float32)
        adj = jax.random.randint(k2, (B, N, N), 0, 5, dtype=jnp.int32)
        a0 = jax.random.normal(k3, (D,), dtype=jnp.float32)
        a1 = jax.random.normal(k4, (D,), dtype=jnp.float32)
        a2 = jax.random.normal(k5, (D,), dtype=jnp.float32)
        a3 = jax.random.normal(k6, (D,), dtype=jnp.float32)
        return {'hidden': hidden, 'adj': adj, 'a0': a0, 'a1': a1, 'a2': a2, 'a3': a3}
    _L0_gnn_all = _L0_gnn_setup()
    _L0_gnn_in = {k: v for k, v in _L0_gnn_all.items() if k in ('a0', 'a1', 'a2', 'a3')}
    del _L0_gnn_all

    def _L0_ffn_setup():
        import jax, jax.numpy as jnp
        import numpy as np
        D_MODEL = 128
        N_EXPERTS = 16
        HIDDEN = 256
        SCALE = 0.02
        key = jax.random.key(seed)
        ks = jax.random.split(key, 5)
        x = jax.random.normal(ks[0], (4, 4096, D_MODEL), dtype=jnp.float32)
        gate_w = jax.random.normal(ks[1], (D_MODEL, N_EXPERTS), dtype=jnp.float32) * SCALE
        gate_b = jnp.zeros((N_EXPERTS,), dtype=jnp.float32)
        w1 = jax.random.normal(ks[2], (N_EXPERTS, D_MODEL, HIDDEN), dtype=jnp.float32) * SCALE
        w2 = jax.random.normal(ks[3], (N_EXPERTS, D_MODEL, HIDDEN), dtype=jnp.float32) * SCALE
        w3 = jax.random.normal(ks[4], (N_EXPERTS, HIDDEN, D_MODEL), dtype=jnp.float32) * SCALE
        return {'x': x, 'gate_w': gate_w, 'gate_b': gate_b, 'w1': w1, 'w2': w2, 'w3': w3}
    _L0_ffn_all = _L0_ffn_setup()
    _L0_ffn_in = {k: v for k, v in _L0_ffn_all.items() if k in ('gate_w', 'gate_b', 'w1', 'w2', 'w3')}
    del _L0_ffn_all
    return {'x': x, 'adj': adj, 'L0_gnn_a0': _L0_gnn_in['a0'], 'L0_gnn_a1': _L0_gnn_in['a1'], 'L0_gnn_a2': _L0_gnn_in['a2'], 'L0_gnn_a3': _L0_gnn_in['a3'], 'L0_ffn_gate_w': _L0_ffn_in['gate_w'], 'L0_ffn_gate_b': _L0_ffn_in['gate_b'], 'L0_ffn_w1': _L0_ffn_in['w1'], 'L0_ffn_w2': _L0_ffn_in['w2'], 'L0_ffn_w3': _L0_ffn_in['w3']}

def reference(x, adj, L0_gnn_a0, L0_gnn_a1, L0_gnn_a2, L0_gnn_a3, L0_ffn_gate_w, L0_ffn_gate_b, L0_ffn_w1, L0_ffn_w2, L0_ffn_w3):
    import jax
    import jax.numpy as jnp

    def _L0_gnn_ref(hidden, adj, a0, a1, a2, a3):
        import jax, jax.numpy as jnp
        import numpy as np
        NEG_INF = -9000000000000000.0
        LEAKY_SLOPE = 0.2

        def edge_score(a):
            s = jnp.einsum('bid,bjd->bij', hidden * a, hidden)
            return jax.nn.leaky_relu(s, LEAKY_SLOPE)
        e0, e1, e2, e3 = (edge_score(a0), edge_score(a1), edge_score(a2), edge_score(a3))
        alpha = jnp.where(adj == 1, e0, NEG_INF)
        alpha = jnp.where(adj == 2, e1, alpha)
        alpha = jnp.where(adj == 3, e2, alpha)
        alpha = jnp.where(adj == 4, e3, alpha)
        alpha = jax.nn.softmax(alpha, axis=-1)
        return jnp.matmul(alpha, hidden)

    def _L0_ffn_ref(x, gate_w, gate_b, w1, w2, w3):
        import jax, jax.numpy as jnp
        import numpy as np
        D_MODEL = 128
        N_EXPERTS = 16
        HIDDEN = 256
        SCALE = 0.02
        n_experts = w1.shape[0]
        logits = jnp.einsum('bsd,de->bse', x, gate_w) + gate_b
        probs = jax.nn.softmax(logits, axis=-1)
        top_probs, top_idx = jax.lax.top_k(probs, 2)
        top_probs = top_probs / jnp.sum(top_probs, axis=-1, keepdims=True)
        dispatch = jnp.sum(jax.nn.one_hot(top_idx, n_experts, dtype=x.dtype) * top_probs[..., None], axis=-2)
        h1 = jnp.einsum('bsd,edh->bseh', x, w1)
        h2 = jnp.einsum('bsd,edh->bseh', x, w2)
        hidden = jax.nn.silu(h1) * h2
        expert_out = jnp.einsum('bseh,eho->bseo', hidden, w3)
        return jnp.einsum('bseo,bse->bso', expert_out, dispatch)
    x = x + _L0_gnn_ref(_layernorm(x, axis=-1), adj, L0_gnn_a0, L0_gnn_a1, L0_gnn_a2, L0_gnn_a3)
    x = x + _L0_ffn_ref(_layernorm(x, axis=-1), L0_ffn_gate_w, L0_ffn_gate_b, L0_ffn_w1, L0_ffn_w2, L0_ffn_w3)
    return x

_drawn_inputs = setup_inputs


def setup_inputs(seed=0):
    import zlib

    import numpy as np

    out = dict(_drawn_inputs(seed))
    spreads = {'L0_ffn_gate_b': (0.0, 0.8)}
    factors = {'L0_ffn_gate_w': 8.0, 'L0_ffn_w1': 8.0, 'L0_ffn_w2': 8.0, 'L0_ffn_w3': 8.0}
    for name, (base, spread) in spreads.items():
        noise = np.random.default_rng([zlib.crc32(name.encode()), seed]).standard_normal(out[name].shape)
        drawn = base * np.exp(spread * noise) if base else spread * noise
        out[name] = jnp.asarray(drawn.astype(out[name].dtype))
    for name, factor in factors.items():
        out[name] = (out[name] * factor).astype(out[name].dtype)
    return out
```

```python
import concourse.bass as bass
from concourse import mybir
from contextlib import ExitStack


def gnn_then_moe(nc: bass.Bass, x, adj, a0, a1, a2, a3, gate_w, gate_b, w1, w2, w3, out):
    f32, bf16, i32, u32, u16 = (mybir.dt.float32, mybir.dt.bfloat16, mybir.dt.int32, mybir.dt.uint32,
                                mybir.dt.uint16)
    ALU, ACT, AX = mybir.AluOpType, mybir.ActivationFunctionType, mybir.AxisListType.X
    ds = bass.ds

    P = 128
    B, N, D = x.shape
    E, _, H = w1.shape
    K = 4
    T = 4
    G = B // T
    C = T * D
    TOP = 2
    EPS = 1e-5
    SLOPE = 0.2
    NEG_INF = -9e15
    TOKENS = B * N
    HC = H // P
    ROW = D + 4
    GATE, DEST = D, D + 1
    REGION = TOKENS + P
    IDLE = E * REGION
    TILES = TOP * TOKENS // P + E
    NOWHERE = 2 * TOP * TOKENS

    dispatched = nc.dram_tensor("dispatched", (IDLE + P, ROW), f32, kind="Internal").ap()
    results = nc.dram_tensor("results", (TOKENS * TOP, D), f32, kind="Internal").ap()
    x_v = x.rearrange("b n d -> n b d")
    adj_v = adj.rearrange("b n m -> n b m")
    out_v = out.rearrange("b n d -> n b d")
    results_v = results.rearrange("(b n r) d -> n b (r d)", n=N, r=TOP)

    ctx = ExitStack()
    with ctx:
        def sb(name, shape, dt=f32):
            return ctx.enter_context(nc.sbuf_tensor(name, shape, dt))

        def pb(name, shape, dt=f32):
            return ctx.enter_context(nc.psum_tensor(name, shape, dt))

        def sem(name):
            return ctx.enter_context(nc.semaphore(name))

        X = sb("X", [P, B * D])
        w12 = sb("w12", [P, E * 2 * H])
        w3s = sb("w3s", [P, E * HC * D])
        ident = sb("ident", [P, P])

        late = sb("late", [P, 2 * TILES * E])
        hTa = late[:, 0:K * C].rearrange("p (k c) -> p k c", k=K)
        score = late[:, K * C:(K + 2) * C].rearrange("p (q c) -> p q c", q=2)
        prob = late[:, (K + 2) * C:(K + 4) * C].rearrange("p (q c) -> p q c", q=2)
        adjt = late[:, (K + 4) * C:(K + 6) * C].bitcast(i32).rearrange("p (q c) -> p q c", q=2)
        mask = late[:, (K + 6) * C:(2 * K + 6) * C].bitcast(u16).rearrange("p (q k c) -> p q k c", q=2, k=K)

        stats1 = sb("stats1", [P, T, 6])
        stats2 = sb("stats2", [P, T, 6])
        mv1 = sb("mv1", [P, 2, T, 2])
        mv2 = sb("mv2", [P, 2, T, 2])
        veps = sb("veps", [P, 2, T])
        veps2 = sb("veps2", [P, 2, T])
        rstd1 = sb("rstd1", [P, 2, T])
        rstd2 = sb("rstd2", [P, 2, T])
        shift1 = sb("shift1", [P, 2, T])
        shift2 = sb("shift2", [P, 2, T])
        minus_half = sb("minus_half", [P, T])
        h = sb("h", [P, 2, C])
        hT = sb("hT", [P, C])
        acol = sb("acol", [P, K])
        probT = sb("probT", [P, C])
        negmax = sb("negmax", [P, 2, T])
        rowsum = sb("rowsum", [P, 2, T])
        rinv = sb("rinv", [P, 2, T])
        stage = sb("stage", [P, 2, T * TOP * ROW])
        x2T = sb("x2T", [P, C])
        gwt = sb("gwt", [P, E])
        gbias = sb("gbias", [P, E])
        logit = sb("logit", [P, T, E])
        best = sb("best", [P, T, 8])
        bestix = sb("bestix", [P, T, 8], u32)
        eiota = sb("eiota", [P, E])
        ebase = sb("ebase", [P, E])
        onehot = sb("onehot", [P, TOP, T * E])
        taken = sb("taken", [P, T * E], bf16)
        takensum = sb("takensum", [P, E])
        before = sb("before", [P, E], bf16)
        pos = sb("pos", [P, T * E])
        hit = sb("hit", [P, TOP, T * E])
        slot = sb("slot", [P, 2, TOP * T], i32)
        gap = sb("gap", [P, T])
        e2 = sb("e2", [P, 2, T])
        den = sb("den", [P, T])
        dest = sb("dest", [P, B * TOP], i32)
        lower = sb("lower", [P, P], bf16)
        ones = sb("ones", [P, P], bf16)

        count = sb("count", [P, E])
        ntile_i = sb("ntile_i", [P, E], i32)
        ntile_s = sb("ntile_s", [P, E], i32)
        ntile = sb("ntile", [P, E])
        zeroE = sb("zeroE", [P, E])
        upto = sb("upto", [P, E])
        tileno = sb("tileno", [P, TILES])
        past = late[0:1, 0:TILES * E].rearrange("p (j e) -> p j e", e=E)
        pastn = late[0:1, TILES * E:2 * TILES * E].rearrange("p (j e) -> p j e", e=E)
        texp = sb("texp", [1, TILES])
        tstart = sb("tstart", [1, TILES])
        trow = sb("trow", [1, TILES])
        trow2 = sb("trow2", [1, TILES])
        texp_i = sb("texp_i", [1, TILES], i32)
        trow_i = sb("trow_i", [1, TILES], i32)
        padrow = sb("padrow", [P, E], i32)
        padf = sb("padf", [P, E])
        padding = sb("padding", [P, ROW])

        TURNS = 4
        S = 8
        xin = sb("xin", [P, S, ROW])
        xT = sb("xT", [P, 2, P])
        silu = sb("silu", [P, 2, H])
        hid = sb("hid", [P, 2, H])
        hidT = sb("hidT", [P, 2, H])
        y = sb("y", [P, S, D])

        ZS = 4
        zin = late[:, 0:ZS * T * TOP * D].rearrange("p (u c) -> p u c", u=ZS)

        bank = [pb(f"bank{i}", [P, 512]) for i in range(4)]
        psS = pb("psS", [P, T, K * D])
        psT, psE, psO, psL = bank
        psH = [psS[:, 0, :], psS[:, 1, :]]
        psHT = [psS[:, 2, :], psS[:, 3, :]]
        psX = [bank[0], bank[1]]
        psY = [bank[2], bank[3]]

        s_const = sem("s_const")
        s_const2 = sem("s_const2")
        s_small = sem("s_small")
        s_x = sem("s_x")
        s_adj = sem("s_adj")
        s_turn2 = sem("s_turn2")
        s_turn = sem("s_turn")
        s_w = sem("s_w")
        s_st1 = sem("s_st1")
        s_ve1 = sem("s_ve1")
        s_ag1 = sem("s_ag1")
        s_rs1 = sem("s_rs1")
        s_sh1 = sem("s_sh1")
        s_h = sem("s_h")
        s_hTp = sem("s_hTp")
        s_hT = sem("s_hT")
        s_hTa = sem("s_hTa")
        s_S = sem("s_S")
        s_mask = sem("s_mask")
        s_sel = sem("s_sel")
        s_selk = [sem(f"s_sel_{k}") for k in range(K - 1)]
        s_nm = sem("s_nm")
        s_leaky = sem("s_leaky")
        s_prob = sem("s_prob")
        s_probTp = sem("s_probTp")
        s_probT = sem("s_probT")
        s_O = sem("s_O")
        s_rinv = sem("s_rinv")
        s_x1 = sem("s_x1")
        s_st2 = sem("s_st2")
        s_ag2 = sem("s_ag2")
        s_ve2 = sem("s_ve2")
        s_rs2 = sem("s_rs2")
        s_sh2 = sem("s_sh2")
        s_x2 = sem("s_x2")
        s_x2Tp = sem("s_x2Tp")
        s_x2T = sem("s_x2T")
        s_L = sem("s_L")
        s_logit = sem("s_logit")
        s_best = sem("s_best")
        s_bestix = sem("s_bestix")
        s_oh = sem("s_oh")
        s_taken = sem("s_taken")
        s_cum = sem("s_cum")
        s_tsum = sem("s_tsum")
        s_before = sem("s_before")
        s_pos = sem("s_pos")
        s_hit = sem("s_hit")
        s_gap = sem("s_gap")
        s_e2 = sem("s_e2")
        s_den = sem("s_den")
        s_g1 = sem("s_g1")
        s_rows = sem("s_rows")
        s_scat = [sem(f"s_scat{i}") for i in range(2)]
        s_pad = sem("s_pad")
        s_count = sem("s_count")
        s_mid = sem("s_mid")
        s_padrow = sem("s_padrow")
        s_table = sem("s_table")
        s_padded = sem("s_padded")
        s_in = [sem(f"s_in{i}") for i in range(S)]
        s_xTp = [sem(f"s_xTp{i}") for i in range(TURNS)]
        s_xT = [sem(f"s_xT{i}") for i in range(TURNS)]
        s_H = [sem(f"s_H{i}") for i in range(TURNS)]
        s_silu = [sem(f"s_silu{i}") for i in range(TURNS)]
        s_hid = [sem(f"s_hid{i}") for i in range(TURNS)]
        s_hidTp = [sem(f"s_hidTp{i}") for i in range(TURNS)]
        s_hidT = [sem(f"s_hidT{i}") for i in range(TURNS)]
        s_Y = [sem(f"s_Y{i}") for i in range(TURNS)]
        s_y = [sem(f"s_y{i}") for i in range(TURNS)]
        s_z = [sem(f"s_z{i}") for i in range(S)]
        s_zin = [sem(f"s_zin{i}") for i in range(ZS)]
        s_add = sem("s_add")
        s_sum = sem("s_sum")
        s_out = sem("s_out")

        CONSTS = 11

        def stage_row(p, t, r):
            at = (t * TOP + r) * ROW
            return stage[:, p, at:at + ROW]

        def stage_v(p):
            return stage[:, p, :].rearrange("p (t r c) -> p t r c", t=T, r=TOP)

        def wait(eng, s, value):
            if not isinstance(value, int) or value > 0:
                eng.wait_ge(s, value)

        def wait_apart(eng, *waits):
            waits = [(s, v if isinstance(v, int) else eng.snap(v)) for s, v in waits]
            eng.wait_ge(s_const, CONSTS)
            for s, value in waits:
                wait(eng, s, value)

        LAST_LAG = 4
        FIRST, END = LAST_LAG + 2, G

        def steps(eng, body):
            def fixed(s):
                body(s, s % 2, lambda lag: 0 <= s - lag < G)
            for s in range(FIRST):
                fixed(s)
            with eng.Fori(FIRST // 2, END // 2) as n:
                for u in range(2):
                    body(n * 2 + u, u, lambda lag: True)
            for s in range(END, G + LAST_LAG):
                fixed(s)

        def tiles(eng, body, ahead):
            def fixed(j):
                body(j // S, j % S, lambda d: 0 <= j + d < TILES)
            for j in range(-ahead, S):
                fixed(j)
            with eng.Fori(1, TILES // S - 1) as n:
                for u in range(S):
                    body(n, u, lambda d: True)
            for j in range(TILES - S, TILES + 2):
                fixed(j)

        def done(eng, sems, n, u, d):
            wait(eng, sems[(u + d) % TURNS], n * (S // TURNS) + (u + d) // TURNS + 1)

        block = ctx.enter_context(nc.Block())

        @block.sync
        def _(sp):
            def load_x(g):
                wait(sp, s_x, g * 16)
                sp.dma_start(X[:, ds(g * C, C)].rearrange("p (t d) -> p t d", t=T),
                             x_v[:, ds(g * T, T), :]).then_inc(s_x, 16)

            def load_adj(g, p):
                wait(sp, s_mask, g - 1)
                sp.sem_inc(s_turn, 1)
                wait(sp, s_adj, g * 16)
                sp.sem_inc(s_turn, 1)
                sp.dma_start(adjt[:, p, :].rearrange("p (t d) -> p t d", t=T),
                             adj_v[:, ds(g * T, T), :]).then_inc(s_adj, 16)

            def load_expert(e):
                sp.dma_start(w12[:, ds(e * 2 * H, H)], w1[ds(e, 1), :, :].rearrange("e d h -> d (e h)")
                             ).then_inc(s_w, 16)
                sp.dma_start(w12[:, ds(e * 2 * H + H, H)], w2[ds(e, 1), :, :].rearrange("e d h -> d (e h)")
                             ).then_inc(s_w, 16)
                sp.dma_start(w3s[:, ds(e * HC * D, HC * D)].rearrange("p (c o) -> p c o", c=HC),
                             w3[ds(e, 1), :, :].rearrange("e (c p) o -> p (e c) o", p=P)).then_inc(s_w, 16)

            load_x(0)
            for k, a in enumerate((a0, a1, a2, a3)):
                sp.dma_start(acol[:, k:k + 1], a.rearrange("(d o) -> d o", o=1)).then_inc(s_small, 16)
            sp.dma_start(gwt[:, :], gate_w).then_inc(s_small, 16)
            sp.dma_start(gbias[:, :], gate_b.partition_broadcast(P)).then_inc(s_small, 16)
            load_x(1)
            for g in range(2):
                load_adj(g, g)
                load_x(g + 2)
            with sp.Fori(0, E // 2) as n:
                for u in range(2):
                    load_adj(n * 2 + (u + 2), u)
                    load_x(n * 2 + (u + 4))
                    load_expert(n * 2 + u)
            with sp.Fori(1 + E // 2, G // 2 - 1) as n:
                for u in range(2):
                    load_adj(n * 2 + u, u)
                    load_x(n * 2 + (u + 2))
            for g in range(G - 2, G):
                load_adj(g, g % 2)

            sp.wait_ge(s_pad, 1)
            sp.dma_start(dispatched[IDLE:IDLE + P, :], padding[:, :]).then_inc(s_padded, 16)
            sp.wait_ge(s_padrow, 1)
            for e in range(E):
                row = sp.value_load(padrow[0:1, e:e + 1], min_val=0, max_val=IDLE - P)
                sp.dma_start(dispatched[ds(row, P), :], padding[:, :]).then_inc(s_padded, 16)

            sp.wait_ge(s_padded, (E + 1) * 16)
            for p in range(2):
                sp.wait_ge(s_scat[p], G // 2 * T * TOP * 16)
            sp.wait_ge(s_table, 1)

            def load_tile(j, u, n):
                wait(sp, s_z[u], n * 16)
                sp.sem_inc(s_turn, 1)
                row = sp.value_load(trow_i[0:1, ds(j, 1)], min_val=0, max_val=IDLE)
                sp.dma_start(xin[:, u, :], dispatched[ds(row, P), :]).then_inc(s_in[u], 16)

            for u in range(S):
                load_tile(u, u, 0)
            with sp.Fori(1, TILES // S) as n:
                for u in range(S):
                    load_tile(n * S + u, u, n)

            for u in range(S):
                sp.wait_ge(s_z[u], TILES // S * 16)

            def load_results(g, u, n):
                if not isinstance(n, int) or n > 0:
                    sp.wait_ge(s_sum, g - ZS + 1)
                sp.dma_start(zin[:, u, :].rearrange("p (t c) -> p t c", t=T),
                             results_v[:, ds(g * T, T), :]).then_inc(s_zin[u], 16)

            for u in range(ZS):
                load_results(u, u, 0)
            with sp.Fori(1, G // ZS) as n:
                for u in range(ZS):
                    load_results(n * ZS + u, u, n)

        @block.gpsimd
        def _(pool):
            nc.gpsimd.memset(ident[:, :], 0.0).then_inc(s_const2, 1)
            nc.gpsimd.memset(ones[:, :], 1.0).then_inc(s_const2, 1)
            nc.gpsimd.memset(minus_half[:, :], -0.5).then_inc(s_const, 1)
            nc.gpsimd.memset(before[:, :], 0.0).then_inc(s_const, 1)
            nc.gpsimd.memset(zeroE[:, :], 0.0).then_inc(s_const, 1)
            nc.gpsimd.memset(padding[:, :], 0.0).then_inc(s_const2, 1)
            nc.gpsimd.memset(stage[:, :, :], 0.0).then_inc(s_const, 1)
            nc.gpsimd.iota(eiota[:, :], [[1, E]], base=0, channel_multiplier=0,
                           allow_small_or_imprecise_dtypes=True).then_inc(s_const, 1)
            nc.gpsimd.iota(tileno[:, :], [[1, TILES]], base=0, channel_multiplier=0,
                           allow_small_or_imprecise_dtypes=True).then_inc(s_const, 1)
            nc.gpsimd.iota(dest[:, :], [[N * TOP, B], [1, TOP]], base=0, channel_multiplier=TOP
                           ).then_inc(s_const, 1)
            pool.wait_ge(s_const2, 3)
            nc.gpsimd.affine_select(out=ident[:, :], in_=ident[:, :], compare_op=ALU.not_equal, fill=1.0,
                                    base=0, pattern=[[-1, P]], channel_multiplier=1).then_inc(s_const, 1)
            nc.gpsimd.affine_select(out=lower[:, :], in_=ones[:, :], compare_op=ALU.is_gt, fill=0.0,
                                    base=0, pattern=[[1, P]], channel_multiplier=-1).then_inc(s_const, 1)
            nc.gpsimd.memset(padding[:, DEST:DEST + 1].bitcast(i32), NOWHERE).then_inc(s_pad, 1)
            pool.wait_ge(s_const, 9)
            nc.gpsimd.tensor_scalar(ebase[:, :], eiota[:, :], float(REGION), None, ALU.mult).then_inc(s_const, 1)
            nc.gpsimd.memset(takensum[:, :], 0.0).then_inc(s_const, 1)

            def step(s, p, on):
                if on(0):
                    pool.wait_ge(s_ve1, s + 1)
                    nc.gpsimd.tensor_tensor(rstd1[:, p, :], veps[:, p, :], minus_half[:, :], ALU.pow
                                            ).then_inc(s_rs1, 1)
                if on(3):
                    g, q = s - 3, 1 - p
                    pool.wait_ge(s_ve2, g + 1)
                    nc.gpsimd.tensor_tensor(rstd2[:, q, :], veps2[:, q, :], minus_half[:, :], ALU.pow
                                            ).then_inc(s_rs2, 1)
                if on(4):
                    g = s - 4
                    pool.wait_ge(s_rows, g + 1)
                    pool.sem_inc(s_turn2, 1)
                    for r in range(TOP):
                        for t in range(T):
                            at = r * T + t
                            pool.indirect_dma_start(
                                dispatched[:, :], bass.IndirectOffsetOnAxis(ap=slot[:, p, at:at + 1], axis=0),
                                stage_row(p, t, r), None).then_inc(s_scat[p], 16)

            steps(pool, step)

            def tile_out(n, u, on):
                if on(-2):
                    done(pool, s_y, n, u, -2)
                    pool.sem_inc(s_turn2, 1)
                    u = (u - 2) % S
                    pool.indirect_dma_start(
                        results[:, :],
                        bass.IndirectOffsetOnAxis(ap=xin[:, u, DEST:DEST + 1].bitcast(i32), axis=0),
                        y[:, u, :], None, bounds_check=TOKENS * TOP - 1, oob_is_err=False
                    ).then_inc(s_z[u], 16)

            tiles(pool, tile_out, 0)

        @block.scalar
        def _(act):
            act.wait_ge(s_small, 6 * 16)
            act.wait_ge(s_const, CONSTS)

            def step(s, p, on):
                q = 1 - p
                if on(4):
                    g = s - 4
                    act.wait_ge(s_sh2, g + 1)
                    wait(act, s_scat[p], 0 if isinstance(g, int) and g < 2 else (g - p) * (T * TOP * 8))
                    for t in range(T):
                        last = nc.scalar.activation(
                            stage_v(p)[:, t, 0, 0:D], X[:, ds(g * C + t * D, D)], ACT.Identity,
                            scale=rstd2[:, p, t:t + 1], bias=shift2[:, p, t:t + 1])
                    last.then_inc(s_x2, 1)
                if on(1):
                    g = s - 1
                    act.wait_ge(s_sh1, g + 1)
                    wait(act, s_O, g - 1)
                    for t in range(T):
                        last = nc.scalar.activation(h[:, q, t * D:(t + 1) * D], X[:, ds(g * C + t * D, D)],
                                                    ACT.Identity, scale=rstd1[:, q, t:t + 1],
                                                    bias=shift1[:, q, t:t + 1])
                    last.then_inc(s_h, 1)
                if on(4):
                    g = s - 4
                    act.wait_ge(s_x2Tp, g + 1)
                    wait(act, s_L, g)
                    nc.scalar.activation(x2T[:, :], psT[:, :], ACT.Copy).then_inc(s_x2T, 1)
                if on(1):
                    g = s - 1
                    act.wait_ge(s_hTp, g + 1)
                    wait(act, s_S, g)
                    nc.scalar.activation(hT[:, :], psT[:, :], ACT.Copy)
                    for k in range(2):
                        last = nc.scalar.activation(hTa[:, k, :], psT[:, :], ACT.Copy, scale=acol[:, k:k + 1])
                    last.then_inc(s_hT, 1)
                if on(2):
                    g = s - 2
                    act.wait_ge(s_nm, g + 1)
                    wait(act, s_rinv, g - 1)
                    for t in range(T):
                        c = slice(t * D, (t + 1) * D)
                        last = nc.scalar.activation(prob[:, p, c], prob[:, p, c], ACT.Exp,
                                                    bias=negmax[:, p, t:t + 1],
                                                    accum_out=rowsum[:, p, t:t + 1])
                    last.then_inc(s_prob, 1)
                    act.wait_ge(s_probTp, g + 1)
                    wait(act, s_O, g)
                    nc.scalar.activation(probT[:, :], psE[:, :], ACT.Copy).then_inc(s_probT, 1)
                if on(4):
                    g = s - 4
                    act.wait_ge(s_gap, g + 1)
                    nc.scalar.activation(e2[:, p, :], gap[:, :], ACT.Exp).then_inc(s_e2, 1)

            steps(act, step)

            def tile(n, u, on):
                w = u % 2
                if on(0):
                    done(act, s_hid, n, u, -2)
                    done(act, s_H, n, u, 0)
                    nc.scalar.activation(silu[:, w, :], psH[w][:, 0:H], ACT.Silu).then_inc(s_silu[u % TURNS], 1)
                if on(1):
                    done(act, s_H, n, u, -1)
                    done(act, s_xTp, n, u, 1)
                    nc.scalar.activation(xT[:, 1 - w, :], psX[1 - w][:, 0:P], ACT.Copy
                                         ).then_inc(s_xT[(u + 1) % TURNS], 1)

            tiles(act, tile, 1)

            def store(g):
                act.wait_ge(s_sum, g + 1)
                act.dma_start(out_v[:, ds(g * T, T), :],
                              X[:, ds(g * C, C)].rearrange("p (t d) -> p t d", t=T)).then_inc(s_out, 16)

            with act.Fori(0, G) as g:
                store(g)
            act.wait_ge(s_out, G * 16)

        @block.vector
        def _(dve):
            v = nc.vector
            dve.wait_ge(s_small, 6 * 16)
            dve.wait_ge(s_const, CONSTS)

            def bc_e(ap, shape):
                return ap.to_broadcast(shape)

            def step(s, p, on):
                q = 1 - p
                if on(4):
                    g = s - 4
                    dve.wait_ge(s_rs2, g + 1)
                    v.scalar_tensor_tensor(shift2[:, p, :], mv2[:, p, :, 0], -1.0, rstd2[:, p, :],
                                           ALU.mult, ALU.mult).then_inc(s_sh2, 1)
                if on(2):
                    dve.wait_ge(s_mask, s - 1)
                    dve.wait_ge(s_S, s - 1)
                if on(0):
                    dve.wait_ge(s_x, (s + 1) * 16)
                    wait(dve, s_ag1, s)
                if on(1):
                    g = s - 1
                    dve.wait_ge(s_rs1, g + 1)
                    v.scalar_tensor_tensor(shift1[:, q, :], mv1[:, q, :, 0], -1.0, rstd1[:, q, :],
                                           ALU.mult, ALU.mult).then_inc(s_sh1, 1)
                for k in range(K):
                    if on(2):
                        if k > 0:
                            wait_apart(dve, (s_selk[k - 1], s - 1))
                        last = v.copy_predicated(score[:, p, :].rearrange("p (t d) -> p t d", t=T),
                                                 mask[:, p, k, :].rearrange("p (t d) -> p t d", t=T),
                                                 psS[:, :, k * D:(k + 1) * D])
                        last.then_inc(s_selk[k] if k < K - 1 else s_sel, 1)
                    if on(0):
                        last = v.bn_stats(stats1[:, k, :], X[:, ds(s * C + k * D, D)])
                if on(0):
                    last.then_inc(s_st1, 1)
                if on(2):
                    g = s - 2
                    dve.wait_ge(s_sel, g + 1)
                    wait(dve, s_probTp, g - 1)
                    v.scalar_tensor_tensor(prob[:, p, :], score[:, p, :], SLOPE, score[:, p, :],
                                           ALU.mult, ALU.max).then_inc(s_leaky, 1)
                if on(0):
                    wait_apart(dve, (s_st1, s + 1))
                    for t in range(T):
                        last = v.bn_aggr(mv1[:, p, t, :], stats1[:, t, :])
                    last.then_inc(s_ag1, 1)
                if on(2):
                    g = s - 2
                    dve.wait_ge(s_leaky, g + 1)
                    v.tensor_reduce(negmax[:, p, :], prob[:, p, :].rearrange("p (t d) -> p t d", t=T),
                                    AX, ALU.max, negate=True).then_inc(s_nm, 1)
                if on(0):
                    dve.wait_ge(s_ag1, s + 1)
                    v.tensor_scalar(veps[:, p, :], mv1[:, p, :, 1], EPS, None, ALU.add).then_inc(s_ve1, 1)
                if on(3):
                    g = s - 3
                    dve.wait_ge(s_prob, g + 1)
                    v.reciprocal(rinv[:, q, :], rowsum[:, q, :]).then_inc(s_rinv, 1)
                if on(1):
                    g = s - 1
                    dve.wait_ge(s_hT, g + 1)
                    for k in range(2, K):
                        last = v.tensor_scalar(hTa[:, k, :], hT[:, :], acol[:, k:k + 1], None, ALU.mult)
                    last.then_inc(s_hTa, 1)
                if on(3):
                    g = s - 3
                    dve.wait_ge(s_O, g + 1)
                    dve.wait_ge(s_rinv, g + 1)
                    for t in range(T):
                        xs = X[:, ds(g * C + t * D, D)]
                        last = v.scalar_tensor_tensor(xs, psO[:, t * D:(t + 1) * D], rinv[:, q, t:t + 1], xs,
                                                      ALU.mult, ALU.add)
                    last.then_inc(s_x1, 1)
                if on(1):
                    g = s - 1
                    dve.wait_ge(s_adj, (g + 1) * 16)
                    wait(dve, s_leaky, g - 1)
                    for k in range(K):
                        v.tensor_scalar(mask[:, q, k, :], adjt[:, q, :], float(k + 1), None, ALU.is_equal)
                    v.tensor_scalar(score[:, q, :], adjt[:, q, :], 0.0, NEG_INF / SLOPE, ALU.mult, ALU.add
                                    ).then_inc(s_mask, 1)
                if on(3):
                    g = s - 3
                    wait_apart(dve, (s_x1, g + 1), (s_ag2, g))
                    for t in range(T):
                        last = v.bn_stats(stats2[:, t, :], X[:, ds(g * C + t * D, D)])
                    last.then_inc(s_st2, 1)
                if on(4):
                    g = s - 4
                    dve.wait_ge(s_L, g + 1)
                    v.tensor_tensor(logit[:, :, :], psL[:, 0:T * E].rearrange("p (t e) -> p t e", t=T),
                                    gbias[:, :].unsqueeze(1).to_broadcast([P, T, E]), ALU.add
                                    ).then_inc(s_logit, 1)
                if on(3):
                    g = s - 3
                    wait_apart(dve, (s_st2, g + 1))
                    for t in range(T):
                        last = v.bn_aggr(mv2[:, q, t, :], stats2[:, t, :])
                    last.then_inc(s_ag2, 1)
                if on(4):
                    g = s - 4
                    wait_apart(dve, (s_logit, g + 1))
                    for t in range(T):
                        last = v.max(best[:, t, :], logit[:, t, :])
                    last.then_inc(s_best, 1)
                if on(3):
                    g = s - 3
                    dve.wait_ge(s_ag2, g + 1)
                    v.tensor_scalar(veps2[:, q, :], mv2[:, q, :, 1], EPS, None, ALU.add).then_inc(s_ve2, 1)
                if on(4):
                    g = s - 4
                    grp = stage_v(p)
                    oh4 = onehot[:, :, :].rearrange("p r (t e) -> p r t e", t=T)
                    wait_apart(dve, (s_best, g + 1))
                    for t in range(T):
                        last = v.max_index(bestix[:, t, :], best[:, t, :], logit[:, t, :])
                    last.then_inc(s_bestix, 1)
                    v.tensor_tensor(gap[:, :], best[:, :, 1], best[:, :, 0], ALU.subtract).then_inc(s_gap, 1)
                    dve.wait_ge(s_x2, g + 1)
                    v.tensor_copy(grp[:, :, 1, 0:D], grp[:, :, 0, 0:D])
                    dve.wait_ge(s_bestix, g + 1)
                    for r in range(TOP):
                        last = v.tensor_tensor(oh4[:, r], eiota[:, :].unsqueeze(1).to_broadcast([P, T, E]),
                                               bestix[:, :, r:r + 1].to_broadcast([P, T, E]), ALU.is_equal)
                    last.then_inc(s_oh, 1)
                    v.tensor_copy(stage[:, p, :].bitcast(i32).rearrange("p (t r c) -> p t r c", t=T, r=TOP)
                                  [:, :, :, DEST], dest[:, ds(g * (T * TOP), T * TOP)]
                                  .rearrange("p (t r) -> p t r", t=T))
                    dve.wait_ge(s_oh, g + 1)
                    v.tensor_tensor(taken[:, :], onehot[:, 0, :], onehot[:, 1, :], ALU.add).then_inc(s_taken, 1)
                    dve.wait_ge(s_e2, g + 1)
                    v.tensor_scalar(den[:, :], e2[:, p, :], 1.0, None, ALU.add).then_inc(s_den, 1)
                    dve.wait_ge(s_taken, g + 1)
                    v.tensor_reduce(takensum[:, :], taken[:, :].rearrange("p (t e) -> p e t", t=T), AX, ALU.add
                                    ).then_inc(s_tsum, 1)
                    dve.wait_ge(s_den, g + 1)
                    v.reciprocal(grp[:, :, 0, GATE], den[:, :]).then_inc(s_g1, 1)
                    dve.wait_ge(s_cum, g + 1)
                    v.tensor_tensor(pos[:, :].rearrange("p (t e) -> p t e", t=T),
                                    psL[:, T * E:2 * T * E].rearrange("p (t e) -> p t e", t=T),
                                    ebase[:, :].unsqueeze(1).to_broadcast([P, T, E]), ALU.add
                                    ).then_inc(s_pos, 1)
                    dve.wait_ge(s_tsum, g + 1)
                    v.tensor_tensor(before[:, :], before[:, :], takensum[:, :], ALU.add).then_inc(s_before, 1)
                    dve.wait_ge(s_g1, g + 1)
                    v.tensor_tensor(grp[:, :, 1, GATE], e2[:, p, :], grp[:, :, 0, GATE], ALU.mult)
                    dve.wait_ge(s_pos, g + 1)
                    v.tensor_tensor(hit[:, :, :], onehot[:, :, :],
                                    pos[:, :].unsqueeze(1).to_broadcast([P, TOP, T * E]), ALU.mult
                                    ).then_inc(s_hit, 1)
                    dve.wait_ge(s_hit, g + 1)
                    with nc.allow_low_precision(reason="whole numbers under 2 ** 24"):
                        v.tensor_reduce(slot[:, p, :], hit[:, :, :].rearrange("p r (t e) -> p (r t) e", t=T),
                                        AX, ALU.add).then_inc(s_rows, 1)

            steps(dve, step)

            links = [0]

            def link(ins):
                links[0] += 1
                ins.then_inc(s_mid, 1)
                dve.wait_ge(s_mid, links[0])

            dve.wait_ge(s_count, 1)
            link(v.tensor_copy(count[:, :], psL[:, 0:E]))
            v.tensor_tensor(padf[:, :], count[:, :], ebase[:, :], ALU.add)
            link(v.tensor_scalar(ntile_i[:, :], count[:, :], float(P - 1), None, ALU.add))
            v.tensor_copy(padrow[:, :], padf[:, :]).then_inc(s_padrow, 1)
            link(v.tensor_scalar(ntile_s[:, :], ntile_i[:, :], P.bit_length() - 1, None, ALU.arith_shift_right))
            link(v.tensor_copy(ntile[:, :], ntile_s[:, :]))
            link(v.tensor_tensor_scan(upto[:, :], ntile[:, :], zeroE[:, :], 0.0, ALU.add, ALU.add))
            link(v.tensor_tensor(past[:, :, :], tileno[0:1, :].unsqueeze(2).to_broadcast([1, TILES, E]),
                                 upto[0:1, :].unsqueeze(1).to_broadcast([1, TILES, E]), ALU.is_ge))
            v.tensor_reduce(texp[:, :], past[:, :, :], AX, ALU.add)
            link(v.tensor_tensor(pastn[:, :, :], past[:, :, :],
                                 ntile[0:1, :].unsqueeze(1).to_broadcast([1, TILES, E]), ALU.mult))
            link(v.tensor_reduce(tstart[:, :], pastn[:, :, :], AX, ALU.add))
            link(v.tensor_tensor(trow[:, :], tileno[0:1, :], tstart[:, :], ALU.subtract))
            v.tensor_scalar(texp_i[:, :], texp[:, :], float(E - 1), None, ALU.min)
            link(v.tensor_scalar(trow2[:, :], trow[:, :], float(P), None, ALU.mult))
            link(v.scalar_tensor_tensor(trow[:, :], texp[:, :], float(REGION), trow2[:, :], ALU.mult, ALU.add))
            v.tensor_scalar(trow_i[:, :], trow[:, :], float(IDLE), None, ALU.min).then_inc(s_table, 1)

            def tile(n, u, on):
                w = u % 2
                if on(0):
                    done(dve, s_hidTp, n, u, -2)
                    done(dve, s_silu, n, u, 0)
                    v.tensor_tensor(hid[:, w, :], silu[:, w, :], psH[w][:, H:2 * H], ALU.mult
                                    ).then_inc(s_hid[u % TURNS], 1)
                if on(-2):
                    k = (u - 2) % S
                    done(dve, s_Y, n, u, -2)
                    v.tensor_scalar(y[:, k, :], psY[w][:, 0:D], xin[:, k, GATE:GATE + 1], None, ALU.mult
                                    ).then_inc(s_y[k % TURNS], 1)
                if on(-1):
                    done(dve, s_Y, n, u, -3)
                    done(dve, s_hidTp, n, u, -1)
                    v.tensor_copy(hidT[:, 1 - w, :], psHT[1 - w][:, 0:H]).then_inc(s_hidT[(u - 1) % TURNS], 1)

            tiles(dve, tile, 0)

            def add_results(g, u, n):
                xs = X[:, ds(g * C, C)].rearrange("p (t d) -> p t d", t=T)
                zs = zin[:, u, :].rearrange("p (t r d) -> p t r d", t=T, r=TOP)
                dve.wait_ge(s_zin[u], (n + 1) * 16)
                v.tensor_tensor(xs, xs, zs[:, :, 0], ALU.add).then_inc(s_add, 1)
                dve.wait_ge(s_add, g + 1)
                v.tensor_tensor(xs, xs, zs[:, :, 1], ALU.add).then_inc(s_sum, 1)

            with dve.Fori(0, G // ZS) as n:
                for u in range(ZS):
                    add_results(n * ZS + u, u, n)

        @block.tensor
        def _(pe):
            mm = nc.tensor.matmul
            pe.wait_ge(s_const, CONSTS)
            pe.wait_ge(s_small, 6 * 16)

            def step(s, p, on):
                q = 1 - p
                if on(4):
                    g = s - 4
                    pe.wait_ge(s_x2, g + 1)
                    pe.wait_ge(s_hT, min(g + 3, G) if isinstance(g, int) else g + 3)
                    for t in range(T):
                        last = nc.tensor.transpose(psT[:, t * D:(t + 1) * D], stage_v(p)[:, t, 0, 0:D],
                                                   ident[:, :])
                    last.then_inc(s_x2Tp, 1)
                if on(1):
                    g = s - 1
                    pe.wait_ge(s_h, g + 1)
                    if on(4):
                        pe.wait_ge(s_x2T, s - 3)
                    elif g > 0:
                        pe.wait_ge(s_hT, g)
                    for t in range(T):
                        last = nc.tensor.transpose(psT[:, t * D:(t + 1) * D], h[:, q, t * D:(t + 1) * D],
                                                   ident[:, :])
                    last.then_inc(s_hTp, 1)
                if on(4):
                    g = s - 4
                    pe.wait_ge(s_x2T, g + 1)
                    wait(pe, s_pos, g)
                    for t in range(T):
                        last = mm(psL[:, t * E:(t + 1) * E], x2T[:, t * D:(t + 1) * D], gwt[:, :],
                                  start=True, stop=True)
                    last.then_inc(s_L, 1)
                if on(2):
                    g = s - 2
                    pe.wait_ge(s_prob, g + 1)
                    wait(pe, s_probT, g)
                    for t in range(T):
                        last = nc.tensor.transpose(psE[:, t * D:(t + 1) * D], prob[:, p, t * D:(t + 1) * D],
                                                   ident[:, :])
                    last.then_inc(s_probTp, 1)
                if on(1):
                    g = s - 1
                    pe.wait_ge(s_hTa, g + 1)
                    wait(pe, s_sel, g)
                    for t in range(T):
                        last = mm(psS[:, t, :], hT[:, t * D:(t + 1) * D], hTa[:, :, t * D:(t + 1) * D],
                                  start=True, stop=True)
                    last.then_inc(s_S, 1)
                if on(2):
                    g = s - 2
                    pe.wait_ge(s_probT, g + 1)
                    wait(pe, s_x1, g)
                    for t in range(T):
                        c = slice(t * D, (t + 1) * D)
                        last = mm(psO[:, c], probT[:, c], h[:, p, c], start=True, stop=True)
                    last.then_inc(s_O, 1)
                if on(4):
                    g = s - 4
                    pe.wait_ge(s_taken, g + 1)
                    wait(pe, s_before, g)
                    at = psL[:, T * E:2 * T * E]
                    mm(at, lower[:, :], taken[:, :], start=True, stop=False)
                    for t in range(T - 1):
                        n = T - 1 - t
                        mm(at[:, (t + 1) * E:].rearrange("p (t e) -> p t e", e=E), ones[:, :],
                           taken[:, t * E:(t + 1) * E].unsqueeze(1).to_broadcast([P, n, E]),
                           start=False, stop=False)
                    mm(at.rearrange("p (t e) -> p t e", e=E), ones[:, :],
                       before[:, :].unsqueeze(1).to_broadcast([P, T, E]), start=False, stop=True
                       ).then_inc(s_cum, 1)

            steps(pe, step)

            pe.wait_ge(s_before, G)
            pe.wait_ge(s_pos, G)
            mm(psL[:, 0:E], ones[:, :], before[:, :], start=True, stop=True).then_inc(s_count, 1)

            pe.wait_ge(s_w, 3 * E * 16)
            pe.wait_ge(s_table, 1)

            def tile(n, u, on):
                w = u % 2
                if on(0):
                    e = pe.value_load(texp_i[0:1, ds(n * S + u, 1)], min_val=0, max_val=E - 1)
                    done(pe, s_hid, n, u, -2)
                    done(pe, s_xT, n, u, 0)
                    mm(psH[w], xT[:, w, :], w12[:, ds(e * (2 * H), 2 * H)], start=True, stop=True
                       ).then_inc(s_H[u % TURNS], 1)
                if on(1):
                    k = (u + 1) % S
                    done(pe, s_xT, n, u, -1)
                    wait(pe, s_in[k], (n + (u + 1) // S + 1) * 16)
                    nc.tensor.transpose(psX[1 - w][:, 0:P], xin[:, k, 0:D], ident[:, :]).then_inc(s_xTp[k % TURNS], 1)
                if on(-2):
                    e = pe.value_load(texp_i[0:1, ds(n * S + (u - 2), 1)], min_val=0, max_val=E - 1)
                    done(pe, s_y, n, u, -4)
                    done(pe, s_hidT, n, u, -2)
                    for c in range(HC):
                        last = mm(psY[w][:, 0:D], hidT[:, w, c * P:(c + 1) * P],
                                  w3s[:, ds(e * (HC * D) + c * D, D)], start=(c == 0), stop=(c == HC - 1))
                    last.then_inc(s_Y[(u - 2) % TURNS], 1)
                if on(-1):
                    done(pe, s_hidT, n, u, -3)
                    done(pe, s_hid, n, u, -1)
                    for c in range(HC):
                        last = nc.tensor.transpose(psHT[1 - w][:, c * P:(c + 1) * P],
                                                   hid[:, 1 - w, c * P:(c + 1) * P], ident[:, :])
                    last.then_inc(s_hidTp[(u - 1) % TURNS], 1)

            tiles(pe, tile, 1)


_INS = ['x', 'adj', 'L0_gnn_a0', 'L0_gnn_a1', 'L0_gnn_a2', 'L0_gnn_a3', 'L0_ffn_gate_w', 'L0_ffn_gate_b',
        'L0_ffn_w1', 'L0_ffn_w2', 'L0_ffn_w3']
_OUTS = [((128, 128, 128), 'float32')]


def kernel(**inputs):
    import numpy as _np
    import concourse.bacc as _bacc
    from concourse import mybir as _mybir
    from concourse.bass_utils import run_bass_kernel_spmd as _run

    nc = _bacc.Bacc("TRN2", target_bir_lowering=False, num_devices=1)
    arrays, args = {}, []
    for name in _INS:
        a = _np.ascontiguousarray(inputs[name])
        arrays[f"in_{name}_dram"] = a
        args.append(nc.dram_tensor(f"in_{name}_dram", a.shape, _mybir.dt.from_np(a.dtype), kind="ExternalInput").ap())
    for i, (shape, dtype) in enumerate(_OUTS):
        dt = _mybir.dt.from_np(_np.dtype(dtype))
        args.append(nc.dram_tensor(f"out_{i}_dram", shape, dt, kind="ExternalOutput").ap())
    gnn_then_moe(nc, *args)
    r = _run(nc, [arrays], core_ids=[0])
    got = tuple(r.results[0][f"out_{i}_dram"] for i in range(len(_OUTS)))
    return got[0]
```
